# Optimizing a Trainium2 kernel written in Bass

```python
import numpy as np
import jax
import jax.numpy as jnp

def _softmax(x, axis=-1):
    return jax.nn.softmax(x, axis=axis)

def _gelu(x):
    return jax.nn.gelu(x, approximate=True)

def _silu(x):
    return jax.nn.silu(x)

def _sigmoid(x):
    return jax.nn.sigmoid(x)

def _layernorm(x, axis=-1, eps=1e-05):
    m = jnp.mean(x, axis=axis, keepdims=True)
    v = jnp.var(x, axis=axis, keepdims=True)
    return (x - m) / jnp.sqrt(v + eps)

def _scatter_add(tgt, idx, src, axis=0):
    return tgt.at[idx].add(src)

def _segment_sum(src, seg, n):
    return jax.ops.segment_sum(src, seg, n)
kernel_name = 'mk_flamingo_gated_d1_seqx_r8_8cf8cb'

def setup_inputs(seed: int=0):
    np.random.seed(seed)
    _w = jnp.asarray

    def _rec_inputs():
        import jax
        import jax.numpy as jnp
        _rk = jax.random.key(seed)
        x = -0.0003929 + 0.9999 * jax.random.normal(jax.random.fold_in(_rk, 1), (32, 64, 512), jnp.float32)
        _lenS = 64 - jax.random.randint(jax.random.fold_in(_rk, 7), (32,), 0, max(1, 64 // 4) + 1, jnp.int32)
        _lenS2 = 64 - jax.random.randint(jax.random.fold_in(_rk, 8), (32,), 0, max(1, 64 // 4) + 1, jnp.int32)
        _ctx_1024P = jax.random.normal(jax.random.fold_in(_rk, 11), (32, 16, 128), jnp.float32)
        _ctx_1024c = jax.random.dirichlet(jax.random.fold_in(_rk, 511), 0.3 * jnp.ones((16,), jnp.float32), (32, 64))
        _ctx_1024t = jnp.einsum('bsk,bkd->bsd', _ctx_1024c, _ctx_1024P)
        _ctx_1024t = _ctx_1024t * jax.lax.rsqrt(jnp.mean(jnp.square(_ctx_1024t)) + 1e-12) * 0.953939
        ctx_1024 = -1.39393e-06 + 0.999914 * (_ctx_1024t + 0.3 * jax.random.normal(jax.random.fold_in(_rk, 611), (32, 64, 128), jnp.float32))
        _g = jax.random.normal(jax.random.fold_in(_rk, 9001), (2, 1), jnp.float32)
        _g = jnp.sign(_g) * jnp.maximum(jnp.abs(_g), 1.0) + (_g == 0) * 1.0
        g_xattn = _g[0]
        g_ffn = _g[1]
        return (x, ctx_1024, g_xattn, g_ffn)
    x, ctx_1024, g_xattn, g_ffn = _rec_inputs()

    def _L0_xattn_setup():
        import jax, jax.numpy as jnp
        import numpy as np
        import math
        DIM_V = 64
        key = jax.random.key(seed)
        k1, k2, k3, k4, k5, k6 = jax.random.split(key, 6)
        B, C, N, M = (8, DIM_V, 512, 128)
        pcd_up = jax.random.normal(k1, (B, C, N), dtype=jnp.float32)
        pcd_down = jax.random.normal(k2, (B, C, M), dtype=jnp.float32)
        s = 1.0 / math.sqrt(C)
        Wq = jax.random.normal(k3, (C, C), dtype=jnp.float32) * s
        Wk = jax.random.normal(k4, (C, C), dtype=jnp.float32) * s
        Wv = jax.random.normal(k5, (C, C), dtype=jnp.float32) * s
        Wskip = jax.random.normal(k6, (C, C), dtype=jnp.float32) * s
        return {'pcd_up': pcd_up, 'pcd_down': pcd_down, 'Wq': Wq, 'Wk': Wk, 'Wv': Wv, 'Wskip': Wskip}
    _L0_xattn_all = _L0_xattn_setup()
    _L0_xattn_in = {k: v for k, v in _L0_xattn_all.items() if k in ('Wq', 'Wk', 'Wv', 'Wskip')}
    del _L0_xattn_all

    def _L0_ffn_setup():
        import jax, jax.numpy as jnp
        import numpy as np
        import math
        IN_DIM = 512
        FEATURES = 512
        BATCH, SEQ = (8, 256)
        key = jax.random.key(seed)
        kx, kk = jax.random.split(key)
        x = jax.random.normal(kx, (BATCH, SEQ, IN_DIM), dtype=jnp.float32)
        kernel = jax.random.randint(kk, (IN_DIM, FEATURES), 0, 2) > 0
        scale = jnp.asarray(1.0 / math.sqrt(IN_DIM), dtype=jnp.float32)
        return {'x': x, 'kernel': kernel, 'scale': scale}
    _L0_ffn_all = _L0_ffn_setup()
    _L0_ffn_in = {k: v for k, v in _L0_ffn_all.items() if k in ('kernel', 'scale')}
    del _L0_ffn_all
    return {'x': x, 'ctx_1024': ctx_1024, 'g_xattn': g_xattn, 'g_ffn': g_ffn, 'L0_xattn_Wq': _L0_xattn_in['Wq'], 'L0_xattn_Wk': _L0_xattn_in['Wk'], 'L0_xattn_Wv': _L0_xattn_in['Wv'], 'L0_xattn_Wskip': _L0_xattn_in['Wskip'], 'L0_ffn_kernel': _L0_ffn_in['kernel'], 'L0_ffn_scale': _L0_ffn_in['scale']}

def reference(x, ctx_1024, g_xattn, g_ffn, L0_xattn_Wq, L0_xattn_Wk, L0_xattn_Wv, L0_xattn_Wskip, L0_ffn_kernel, L0_ffn_scale):
    import jax
    import jax.numpy as jnp

    def _L0_xattn_ref(pcd_up, pcd_down, Wq, Wk, Wv, Wskip):
        import jax, jax.numpy as jnp
        import numpy as np
        import math
        DIM_V = 64
        q = jnp.einsum('oc,bcn->bon', Wq, pcd_up)
        k = jnp.einsum('oc,bcm->bom', Wk, pcd_down)
        v = jnp.einsum('oc,bcm->bom', Wv, pcd_down)
        C = q.shape[1]
        scale = jnp.sqrt(jnp.asarray(C, dtype=q.dtype))
        energy = jnp.einsum('bcn,bcm->bnm', q, k) / scale
        attention = jax.nn.softmax(energy, axis=-1)
        x = jnp.einsum('bnm,bcm->bcn', attention, v)
        skip = jnp.einsum('oc,bcn->bon', Wskip, pcd_up)
        return skip + x

    def _L0_ffn_ref(x, kernel, scale):
        import jax, jax.numpy as jnp
        import numpy as np
        import math
        IN_DIM = 512
        FEATURES = 512
        BATCH, SEQ = (8, 256)
        w = kernel.astype(x.dtype) * 2.0 - 1.0
        return scale * jnp.einsum('bsi,if->bsf', x, w)
    x = x + jnp.tanh(g_xattn[0]) * _L0_xattn_ref(_layernorm(x, axis=-1), ctx_1024, L0_xattn_Wq, L0_xattn_Wk, L0_xattn_Wv, L0_xattn_Wskip)
    x = x + jnp.tanh(g_ffn[0]) * _L0_ffn_ref(_layernorm(x, axis=-1), L0_ffn_kernel, L0_ffn_scale)
    return x

_drawn_inputs = setup_inputs


def setup_inputs(seed=0):
    import zlib

    import numpy as np

    out = dict(_drawn_inputs(seed))
    spreads = {}
    factors = {}
    for name, (base, spread) in spreads.items():
        noise = np.random.default_rng([zlib.crc32(name.encode()), seed]).standard_normal(out[name].shape)
        drawn = base * np.exp(spread * noise) if base else spread * noise
        out[name] = jnp.asarray(drawn.astype(out[name].dtype))
    for name, factor in factors.items():
        out[name] = (out[name] * factor).astype(out[name].dtype)
    return out
```

```python
from contextlib import ExitStack

import concourse.bass as bass
from concourse import mybir

F32 = mybir.dt.float32
F16 = mybir.dt.float16
U8 = mybir.dt.uint8
ALU = mybir.AluOpType
ACT = mybir.ActivationFunctionType
AX_X = mybir.AxisListType.X
P = 128
EPS = 1e-5


def live(count):
    return not isinstance(count, int) or count > 0


def flamingo_gated_block(nc, x, ctx, g_xattn, g_ffn, Wq, Wk, Wv, Wskip, signs, scale, out):
    B, C, N = x.shape
    M = ctx.shape[2]
    PAIRS = B * C // P
    NT = N // P
    assert 2 * C == P and M == P and N == 4 * P and PAIRS % 2 == 0 and PAIRS >= 8

    x_pairs = x.rearrange("(t b) c n -> (b c) t n", b=2)
    ctx_pairs = ctx.rearrange("(t b) c m -> (b c) t m", b=2)
    out_pairs = out.rearrange("(t b) c n -> (b c) t n", b=2)
    halves = [slice(0, C), slice(C, 2 * C)]

    with ExitStack() as stack:
        def sbuf(name, shape, dtype=F32):
            return stack.enter_context(nc.sbuf_tensor(name, shape, dtype))

        def bank(name, shape):
            return stack.enter_context(nc.psum_tensor(name, shape, F32))

        def sem(name):
            return stack.enter_context(nc.semaphore(name))

        ident = sbuf("ident", [P, P])
        minus_half = sbuf("minus_half", [P, 2])
        wq_sb = sbuf("wq_sb", [C, C])
        wk_sb = sbuf("wk_sb", [C, C])
        wskip_twice = sbuf("wskip_twice", [C, 2, C])
        wv_twice = sbuf("wv_twice", [C, 2, C])
        gates = sbuf("gates", [P, 4])
        tanh_gates = sbuf("tanh_gates", [P, 2])
        ffn_gain = sbuf("ffn_gain", [P, 1])
        signs_raw = sbuf("signs_raw", [P, NT, N], U8)
        signs_sb = sbuf("signs_sb", [P, NT, N], F16)
        score_w = sbuf("score_w", [P, P])
        skip_w = sbuf("skip_w", [P, P])
        value_w = sbuf("value_w", [P, P])
        x_all = sbuf("x_all", [P, PAIRS, N])
        ctx_in = sbuf("ctx_in", [P, 2, M])
        keys_values = sbuf("keys_values", [P, 2, 2, P])
        up = sbuf("up", [P, 2, N])
        x1 = sbuf("x1", [P, 2, N])
        minus_max = sbuf("minus_max", [P, 2, NT])
        sums = sbuf("sums", [P, 2, NT])
        inv_sums = sbuf("inv_sums", [P, 2, NT])
        probs = sbuf("probs", [P, 2, NT, M])
        probs_t = sbuf("probs_t", [P, 2, N])
        moments = sbuf("moments", [P, 2, 6])
        mean_var = sbuf("mean_var", [P, 2, 2])
        var_eps = sbuf("var_eps", [P, 2])
        minus_mean = sbuf("minus_mean", [P, 2])
        rstd = sbuf("rstd", [P, 2])
        shift = sbuf("shift", [P, 2])
        x1_normed = sbuf("x1_normed", [P, NT, P])
        turned_hi = sbuf("turned_hi", [P, NT, P], F16)
        turned_lo = sbuf("turned_lo", [P, NT, P], F16)

        ps_scores = [bank(f"ps_scores{b}", [P, NT, M]) for b in range(2)]
        ps_probs_t = [bank(f"ps_probs_t{b}", [P, N]) for b in range(2)]
        ps_attn = bank("ps_attn", [P, N])
        ps_turned = bank("ps_turned", [P, NT, P])
        ps_ffn = bank("ps_ffn", [P, N])
        ps_kv = bank("ps_kv", [P, 4, P])

        w_loaded = sem("w_loaded")
        gates_loaded = sem("gates_loaded")
        signs_loaded = sem("signs_loaded")
        x_loaded = [sem(f"x_loaded{k}") for k in range(2)]
        ctx_loaded = [sem(f"ctx_loaded{k}") for k in range(2)]
        stored = sem("stored")
        consts_set = sem("consts_set")
        ident_ready = sem("ident_ready")
        tanh_ready = sem("tanh_ready")
        gain_ready = sem("gain_ready")
        w_products = sem("w_products")
        w_ready = sem("w_ready")
        signs_ready = sem("signs_ready")
        kv_made = sem("kv_made")
        attn_made = sem("attn_made")
        ffn_made = sem("ffn_made")
        x1_turned = sem("x1_turned")
        kv_ready = sem("kv_ready")
        up_ready = sem("up_ready")
        hi_ready = sem("hi_ready")
        probs_t0_ready = sem("probs_t0_ready")
        probs_t1_ready = sem("probs_t1_ready")
        lo_ready = sem("lo_ready")
        x_measured = sem("x_measured")
        x1_ready = sem("x1_ready")
        x1_measured = sem("x1_measured")
        out_ready = sem("out_ready")
        x1_normed_ready = sem("x1_normed_ready")
        scores_made = sem("scores_made")
        max_ready = sem("max_ready")
        exp_ready = sem("exp_ready")
        inv_ready = sem("inv_ready")
        probs_ready = sem("probs_ready")
        probs_turned = sem("probs_turned")
        aggregated = sem("aggregated")
        stats_ready = sem("stats_ready")
        rstd_made = sem("rstd_made")
        norm_ready = sem("norm_ready")
        moments_seen = sem("moments_seen")
        norm_seen = sem("norm_seen")

        block = stack.enter_context(nc.Block())

        def norms_in(t):
            if isinstance(t, int):
                return slice(0 if t + 1 < PAIRS else 1, 2 if t >= 1 else 1)
            return slice(0, 2)

        @block.sync
        def _(sp):
            def load(t, par):
                if live(t - 1):
                    sp.wait_ge(x_measured, t - 1)
                sp.dma_start(x_all[:, t, :], x_pairs[:, t, :]).then_inc(x_loaded[par], 16)
                if live(t - 1):
                    sp.wait_ge(kv_made, t - 1)
                sp.dma_start(ctx_in[:, par, :], ctx_pairs[:, t, :]).then_inc(ctx_loaded[par], 16)

            def store(t):
                sp.wait_ge(out_ready, t + 1)
                sp.dma_start(out_pairs[:, t, :], x_all[:, t, :]).then_inc(stored, 16)

            load(0, 0)
            sp.dma_start(wk_sb[:, :], Wk).then_inc(w_loaded, 16)
            sp.dma_start(wq_sb[:, :], Wq).then_inc(w_loaded, 16)
            for b in range(2):
                sp.dma_start(wv_twice[:, b, :], Wv).then_inc(w_loaded, 16)
                sp.dma_start(wskip_twice[:, b, :], Wskip).then_inc(w_loaded, 16)
            load(1, 1)
            sp.dma_start(signs_raw[:, :, :], signs.rearrange("(k p) f -> p k f", p=P)).then_inc(signs_loaded, 16)
            for t in range(0, 2):
                load(t + 2, t % 2)
            with sp.Fori(2, PAIRS - 3, 2) as t:
                for par in range(2):
                    load(t + par + 2, par)
                    store(t + par - 2)
            for t in range(PAIRS - 4, PAIRS):
                store(t)
            sp.wait_ge(stored, 16 * PAIRS)

        @block.tensor
        def _(pe):
            def kv(t, par):
                pe.wait_ge(ctx_loaded[par], 16 * (t // 2 + 1) if isinstance(t, int) else (t - par) * 8 + 16)
                if live(t):
                    pe.wait_ge(kv_ready, t)
                pe.matmul(ps_kv[:, 0, :], score_w[:, :], ctx_in[:, par, :], start=True, stop=True)
                pe.matmul(ps_kv[:, 1, :], ctx_in[:, par, :], value_w[:, :], start=True, stop=True).then_inc(kv_made, 1)

            def scores(t, par):
                pe.wait_ge(up_ready, t + 1)
                pe.wait_ge(kv_ready, t + 1)
                for b, half in enumerate(halves):
                    if live(2 * t + b - 1):
                        pe.wait_ge(exp_ready, 2 * t + b - 1)
                    for j in range(NT):
                        mm = pe.matmul(ps_scores[b][:, j, :], up[half, par, j * P:(j + 1) * P],
                                       keys_values[half, par, 0, :], start=True, stop=True)
                    mm.then_inc(scores_made, 1)

            def values(t, par):
                pe.wait_ge(probs_t0_ready, t + 1)
                pe.wait_ge(probs_t1_ready, t + 1)
                for b, half in enumerate(halves):
                    mm = pe.matmul(ps_attn[half, :], keys_values[:, par, 1, half], probs_t[:, b, :],
                                   start=False, stop=True, skip_group_check=True)
                mm.then_inc(attn_made, 1)

            def ffn(t):
                pe.wait_ge(hi_ready, t + 1)
                pe.wait_ge(lo_ready, t + 1)
                if live(t):
                    pe.wait_ge(out_ready, t)
                for part in (turned_hi, turned_lo):
                    for k in range(NT):
                        mm = pe.matmul(ps_ffn[:, :], part[:, k, :], signs_sb[:, k, :],
                                       start=part is turned_hi and k == 0, stop=part is turned_lo and k == NT - 1)
                mm.then_inc(ffn_made, 1)

            def skip(t, par):
                if live(t):
                    pe.wait_ge(x1_ready, t)
                pe.matmul(ps_attn[:, :], skip_w[:, :], up[:, par, :], start=True, stop=False, skip_group_check=True)

            def turn_probs(t):
                for b in range(2):
                    pe.wait_ge(probs_ready, 2 * t + b + 1)
                    for j in range(NT):
                        mm = pe.transpose(ps_probs_t[b][:, j * P:(j + 1) * P], probs[:, b, j, :], ident[:, :])
                    mm.then_inc(probs_turned, 1)

            def turn_x1(t):
                pe.wait_ge(x1_normed_ready, t + 1)
                for k in range(NT):
                    mm = pe.transpose(ps_turned[:, k, :], x1_normed[:, k, :], ident[:, :])
                mm.then_inc(x1_turned, 1)

            def step(t, par, peeled=True):
                now = not peeled or 0 <= t < PAIRS
                before = not peeled or 1 <= t <= PAIRS
                if now:
                    scores(t, par)
                if not peeled or t + 1 < PAIRS:
                    kv(t + 1, 1 - par)
                if before:
                    values(t - 1, 1 - par)
                if not peeled or t >= 2:
                    ffn(t - 2)
                if now:
                    skip(t, par)
                    turn_probs(t)
                if before:
                    turn_x1(t - 1)

            pe.wait_ge(w_loaded, 16 * 6)
            for b, half in enumerate(halves):
                pe.matmul(ps_scores[0][half, 0, half], wk_sb[:, :], wq_sb[:, :], start=True, stop=True)
            pe.wait_ge(ident_ready, 2)
            pe.transpose(ps_scores[0][:, 1, 0:C], wskip_twice[:, :, :].rearrange("o b c -> o (b c)"), ident[0:C, 0:C])
            pe.transpose(ps_scores[0][:, 2, 0:C], wv_twice[:, :, :].rearrange("o b c -> o (b c)"),
                         ident[0:C, 0:C]).then_inc(w_products, 1)
            pe.wait_ge(w_ready, 1)
            kv(0, 0)
            for t in range(0, 2):
                step(t, t % 2)
            pe.wait_ge(signs_ready, 1)
            step(2, 0)
            with pe.Fori(3, PAIRS - 2, 2) as t:
                for odd in range(2):
                    step(t + odd, (1 + odd) % 2, peeled=False)
            for t in range(PAIRS - 1, PAIRS + 2):
                step(t, t % 2)

        @block.scalar
        def _(act):
            def head(t):
                act.wait_ge(x1_turned, t + 1)
                if live(t):
                    act.wait_ge(ffn_made, t)
                nc.scalar.activation(turned_hi[:, :, :], ps_turned[:, :, :], ACT.Copy).then_inc(hi_ready, 1)

            def exponentials(t, b):
                act.wait_ge(max_ready, 2 * t + b + 1)
                if live(2 * t + b - 1):
                    act.wait_ge(probs_turned, 2 * t + b - 1)
                for j in range(NT):
                    last = nc.scalar.activation(probs[:, b, j, :], ps_scores[b][:, j, :], ACT.Exp,
                                                bias=minus_max[:, b, j:j + 1], accum_out=sums[:, b, j:j + 1])
                last.then_inc(exp_ready, 1)

            def copy_kv(t, par):
                act.wait_ge(kv_made, t + 1)
                if live(t - 1):
                    act.wait_ge(attn_made, t - 1)
                nc.scalar.activation(keys_values[:, par, :, :], ps_kv[:, 0:2, :], ACT.Copy).then_inc(kv_ready, 1)

            def normalize(t, par):
                act.wait_ge(norm_ready, t + 1)
                nc.scalar.activation(up[:, par, :], x_all[:, t, :], ACT.Identity, bias=shift[:, 0:1],
                                     scale=rstd[:, 0:1]).then_inc(up_ready, 1)

            def step(t, par, peeled=True):
                if not peeled or t >= 2:
                    head(t - 2)
                if not peeled or 0 <= t < PAIRS:
                    exponentials(t, 0)
                    exponentials(t, 1)
                if not peeled or t + 1 < PAIRS:
                    copy_kv(t + 1, 1 - par)
                    normalize(t + 1, 1 - par)
                if not peeled or 0 <= t < PAIRS:
                    act.wait_ge(probs_turned, 2 * t + 1)
                    if live(t):
                        act.wait_ge(attn_made, t)
                    nc.scalar.activation(probs_t[:, 0, :], ps_probs_t[0][:, :], ACT.Copy).then_inc(probs_t0_ready, 1)

            act.dma_start(gates[:, 0:1], g_xattn[None, :].broadcast_to([P, 1])).then_inc(gates_loaded, 16)
            act.dma_start(gates[:, 1:2], g_ffn[None, :].broadcast_to([P, 1])).then_inc(gates_loaded, 16)
            act.dma_start(gates[:, 2:3], scale[None, :].broadcast_to([P, 1])).then_inc(gates_loaded, 16)
            act.wait_ge(gates_loaded, 48)
            nc.scalar.activation(tanh_gates[:, :], gates[:, 0:2], ACT.Tanh).then_inc(tanh_ready, 1)
            for t in range(-1, 3):
                step(t, t % 2)
            with act.Fori(3, PAIRS - 2, 2) as t:
                for odd in range(2):
                    step(t + odd, (1 + odd) % 2, peeled=False)
            for t in range(PAIRS - 1, PAIRS + 2):
                step(t, t % 2)

        @block.vector
        def _(dve):
            def rest(t):
                dve.wait_ge(hi_ready, t + 1)
                nc.vector.tensor_tensor(turned_lo[:, :, :], ps_turned[:, :, :], turned_hi[:, :, :],
                                        ALU.subtract).then_inc(lo_ready, 1)

            def maxima(t, b):
                dve.wait_ge(scores_made, 2 * t + b + 1)
                nc.vector.tensor_reduce(minus_max[:, b, :], ps_scores[b][:, :, :], AX_X, ALU.max,
                                        negate=True).then_inc(max_ready, 1)

            def measure_x(t, par):
                dve.wait_ge(x_loaded[par], 16 * (t // 2 + 1) if isinstance(t, int) else (t - par) * 8 + 16)
                nc.vector.bn_stats(moments[:, 0, :], x_all[:, t, :]).then_inc(x_measured, 1)

            def residual(t, par):
                dve.wait_ge(attn_made, t + 1)
                nc.vector.tensor_tensor(x1[:, par, :], ps_attn[:, :], x_all[:, t, :], ALU.add).then_inc(x1_ready, 1)
                dve.wait_ge(x1_ready, t + 1)
                nc.vector.bn_stats(moments[:, 1, :], x1[:, par, :]).then_inc(x1_measured, 1)

            def statistics(t):
                cols = norms_in(t)
                if cols.start == 0:
                    dve.wait_ge(x_measured, t + 2)
                if cols.stop == 2:
                    dve.wait_ge(x1_measured, t)
                dve.sem_inc(moments_seen, 1)
                if cols.start == 0:
                    last = nc.vector.bn_aggr(mean_var[:, 0, :], moments[:, 0, :])
                if cols.stop == 2:
                    last = nc.vector.bn_aggr(mean_var[:, 1, :], moments[:, 1, :])
                last.then_inc(aggregated, 1)
                dve.wait_ge(aggregated, t + 2)
                nc.vector.tensor_scalar(minus_mean[:, cols], mean_var[:, cols, 0], -1.0, None, ALU.mult)
                nc.vector.tensor_scalar(var_eps[:, cols], mean_var[:, cols, 1], EPS, None,
                                        ALU.add).then_inc(stats_ready, 1)

            def invert(t, b):
                dve.wait_ge(exp_ready, 2 * t + b + 1)
                nc.vector.reciprocal(inv_sums[:, b, :], sums[:, b, :]).then_inc(inv_ready, 1)

            def result(t, par):
                dve.wait_ge(ffn_made, t + 1)
                nc.vector.scalar_tensor_tensor(out=x_all[:, t, :], in0=ps_ffn[:, :], scalar=ffn_gain[:, 0:1],
                                               in1=x1[:, par, :], op0=ALU.mult, op1=ALU.add).then_inc(out_ready, 1)

            def step(t, par, peeled=True):
                now = not peeled or 0 <= t < PAIRS
                late = not peeled or t >= 2
                if late:
                    rest(t - 2)
                if now:
                    maxima(t, 0)
                    maxima(t, 1)
                if not peeled or t + 1 < PAIRS:
                    measure_x(t + 1, 1 - par)
                if not peeled or 1 <= t <= PAIRS:
                    residual(t - 1, 1 - par)
                if not peeled or t <= PAIRS:
                    statistics(t)
                if now:
                    invert(t, 0)
                if late:
                    result(t - 2, par)
                if now:
                    invert(t, 1)
                    dve.wait_ge(probs_turned, 2 * t + 2)
                    if live(t):
                        dve.wait_ge(attn_made, t)
                    nc.vector.tensor_copy(probs_t[:, 1, :], ps_probs_t[1][:, :]).then_inc(probs_t1_ready, 1)

            nc.vector.memset(minus_half[:, :], -0.5).then_inc(consts_set, 1)
            for w in (score_w, skip_w, value_w):
                nc.vector.memset(w[:, :], 0.0).then_inc(consts_set, 1)
            step(-1, 1)
            dve.wait_ge(tanh_ready, 1)
            nc.vector.tensor_tensor(ffn_gain[:, :], tanh_gates[:, 1:2], gates[:, 2:3], ALU.mult).then_inc(gain_ready, 1)
            dve.wait_ge(w_products, 1)
            dve.wait_ge(consts_set, 4)
            for half in halves:
                nc.vector.tensor_scalar(score_w[half, half], ps_scores[0][half, 0, half], float(C) ** -0.5, None,
                                        ALU.mult)
                nc.vector.tensor_scalar(skip_w[half, half], ps_scores[0][half, 1, 0:C], tanh_gates[half, 0:1], None,
                                        ALU.mult)
                last = nc.vector.tensor_scalar(value_w[half, half], ps_scores[0][half, 2, 0:C],
                                               tanh_gates[half, 0:1], None, ALU.mult)
            last.then_inc(w_ready, 1)
            dve.wait_ge(gain_ready, 1)
            for t in range(0, 3):
                step(t, t % 2)
            with dve.Fori(3, PAIRS - 2, 2) as t:
                for odd in range(2):
                    step(t + odd, (1 + odd) % 2, peeled=False)
            for t in range(PAIRS - 1, PAIRS + 2):
                step(t, t % 2)

        @block.gpsimd
        def _(pool):
            def norm_factors(t):
                cols = norms_in(t)
                pool.wait_ge(stats_ready, t + 2)
                nc.gpsimd.tensor_tensor(rstd[:, cols], var_eps[:, cols], minus_half[:, cols],
                                        ALU.pow).then_inc(rstd_made, 1)
                pool.wait_ge(rstd_made, t + 2)
                nc.gpsimd.tensor_tensor(shift[:, cols], minus_mean[:, cols], rstd[:, cols],
                                        ALU.mult).then_inc(norm_ready, 1)

            def normalize_x1(t, par):
                pool.wait_ge(norm_ready, t + 3)
                if live(t):
                    pool.wait_ge(x1_turned, t)
                pool.sem_inc(norm_seen, 1)
                nc.gpsimd.tensor_scalar(x1_normed[:, :, :].rearrange("p k n -> p (k n)"), x1[:, par, :],
                                        rstd[:, 1:2], shift[:, 1:2], ALU.mult, ALU.add).then_inc(x1_normed_ready, 1)

            def divide(t, b):
                pool.wait_ge(inv_ready, 2 * t + b + 1)
                nc.gpsimd.tensor_tensor(probs[:, b, :, :], probs[:, b, :, :],
                                        inv_sums[:, b, :, None].broadcast_to([P, NT, M]),
                                        ALU.mult).then_inc(probs_ready, 1)

            def step(t, par, peeled=True):
                now = not peeled or 0 <= t < PAIRS
                if now:
                    divide(t, 0)
                if not peeled or t <= PAIRS:
                    norm_factors(t)
                if not peeled or 1 <= t <= PAIRS:
                    normalize_x1(t - 1, 1 - par)
                if now:
                    divide(t, 1)

            nc.gpsimd.memset(ident[:, :], 0.0).then_inc(ident_ready, 1)
            pool.wait_ge(ident_ready, 1)
            nc.gpsimd.affine_select(out=ident[:, :], in_=ident[:, :], compare_op=ALU.not_equal, fill=1.0, base=0,
                                    pattern=[[-1, P]], channel_multiplier=1).then_inc(ident_ready, 1)
            pool.wait_ge(consts_set, 1)
            step(-1, 1)
            pool.wait_ge(signs_loaded, 16)
            for k in range(NT):
                last = nc.gpsimd.tensor_scalar(signs_sb[:, k, :], signs_raw[:, k, :], 2.0, -1.0, ALU.mult, ALU.add)
            last.then_inc(signs_ready, 1)
            for t in range(0, 3):
                step(t, t % 2)
            with pool.Fori(3, PAIRS - 2, 2) as t:
                for odd in range(2):
                    step(t + odd, (1 + odd) % 2, peeled=False)
            for t in range(PAIRS - 1, PAIRS + 2):
                step(t, t % 2)


_INS = ["x", "ctx_1024", "g_xattn", "g_ffn", "L0_xattn_Wq", "L0_xattn_Wk", "L0_xattn_Wv", "L0_xattn_Wskip",
        "L0_ffn_kernel", "L0_ffn_scale"]


def kernel(**inputs):
    import numpy as np
    import concourse.bacc as bacc
    from concourse.bass_utils import run_bass_kernel_spmd as run

    nc = bacc.Bacc("TRN2", target_bir_lowering=False, num_devices=1)
    arrays, args = {}, []
    for name in _INS:
        a = np.ascontiguousarray(inputs[name])
        arrays[f"in_{name}"] = a
        args.append(nc.dram_tensor(f"in_{name}", a.shape, mybir.dt.from_np(a.dtype), kind="ExternalInput").ap())
    shape = inputs["x"].shape
    args.append(nc.dram_tensor("out", shape, F32, kind="ExternalOutput").ap())
    flamingo_gated_block(nc, *args)
    return run(nc, [arrays], core_ids=[0]).results[0]["out"]
```

```python
from contextlib import ExitStack

import concourse.bass as bass
from concourse import mybir

F32 = mybir.dt.float32
F16 = mybir.dt.float16
U8 = mybir.dt.uint8
ALU = mybir.AluOpType
ACT = mybir.ActivationFunctionType
AX_X = mybir.AxisListType.X
P = 128
EPS = 1e-5


def live(count):
    return not isinstance(count, int) or count > 0


def flamingo_gated_block(nc, x, ctx, g_xattn, g_ffn, Wq, Wk, Wv, Wskip, signs, scale, out):
    B, C, N = x.shape
    M = ctx.shape[2]
    PAIRS = B * C // P
    NT = N // P
    assert 2 * C == P and M == P and N == 4 * P and PAIRS % 2 == 0 and PAIRS >= 8

    x_pairs = x.rearrange("(t b) c n -> (b c) t n", b=2)
    ctx_pairs = ctx.rearrange("(t b) c m -> (b c) t m", b=2)
    out_pairs = out.rearrange("(t b) c n -> (b c) t n", b=2)
    halves = [slice(0, C), slice(C, 2 * C)]

    with ExitStack() as stack:
        def sbuf(name, shape, dtype=F32):
            return stack.enter_context(nc.sbuf_tensor(name, shape, dtype))

        def bank(name, shape):
            return stack.enter_context(nc.psum_tensor(name, shape, F32))

        def sem(name):
            return stack.enter_context(nc.semaphore(name))

        ident = sbuf("ident", [P, P])
        minus_half = sbuf("minus_half", [P, 2])
        wq_sb = sbuf("wq_sb", [C, C])
        wk_sb = sbuf("wk_sb", [C, C])
        wskip_twice = sbuf("wskip_twice", [C, 2, C])
        wv_twice = sbuf("wv_twice", [C, 2, C])
        gates = sbuf("gates", [P, 4])
        tanh_gates = sbuf("tanh_gates", [P, 2])
        ffn_gain = sbuf("ffn_gain", [P, 1])
        signs_raw = sbuf("signs_raw", [P, NT, N], U8)
        signs_sb = sbuf("signs_sb", [P, NT, N], F16)
        score_w = sbuf("score_w", [P, P])
        skip_w = sbuf("skip_w", [P, P])
        value_w = sbuf("value_w", [P, P])
        x_all = sbuf("x_all", [P, PAIRS, N])
        ctx_in = sbuf("ctx_in", [P, 2, M])
        keys_values = sbuf("keys_values", [P, 2, 2, P])
        up = sbuf("up", [P, 2, N])
        x1 = sbuf("x1", [P, 2, N])
        minus_max = sbuf("minus_max", [P, 2, NT])
        sums = sbuf("sums", [P, 2, NT])
        inv_sums = sbuf("inv_sums", [P, 2, NT])
        probs = sbuf("probs", [P, 2, 2, NT, M])
        probs_t = sbuf("probs_t", [P, 2, 2, N])
        moments = sbuf("moments", [P, 2, 6])
        mean_var = sbuf("mean_var", [P, 2, 2])
        var_eps = sbuf("var_eps", [P, 2])
        minus_mean = sbuf("minus_mean", [P, 2])
        rstd = sbuf("rstd", [P, 2])
        shift = sbuf("shift", [P, 2])
        x1_normed = sbuf("x1_normed", [P, NT, P])
        turned_hi = sbuf("turned_hi", [P, NT, P], F16)
        turned_lo = sbuf("turned_lo", [P, NT, P], F16)

        ps_scores = [bank(f"ps_scores{b}", [P, NT, M]) for b in range(2)]
        ps_probs_t = [bank(f"ps_probs_t{b}", [P, N]) for b in range(2)]
        ps_attn = bank("ps_attn", [P, N])
        ps_turned = bank("ps_turned", [P, NT, P])
        ps_ffn = bank("ps_ffn", [P, N])
        ps_kv = bank("ps_kv", [P, 4, P])

        w_loaded = sem("w_loaded")
        gates_loaded = sem("gates_loaded")
        signs_loaded = sem("signs_loaded")
        x_loaded = [sem(f"x_loaded{k}") for k in range(2)]
        ctx_loaded = [sem(f"ctx_loaded{k}") for k in range(2)]
        stored = sem("stored")
        consts_set = sem("consts_set")
        ident_ready = sem("ident_ready")
        tanh_ready = sem("tanh_ready")
        gain_ready = sem("gain_ready")
        w_products = sem("w_products")
        w_ready = sem("w_ready")
        signs_ready = sem("signs_ready")
        kv_made = sem("kv_made")
        attn_made = sem("attn_made")
        ffn_made = sem("ffn_made")
        x1_turned = sem("x1_turned")
        kv_ready = sem("kv_ready")
        up_ready = sem("up_ready")
        hi_ready = sem("hi_ready")
        probs_t0_ready = sem("probs_t0_ready")
        probs_t1_ready = sem("probs_t1_ready")
        lo_ready = sem("lo_ready")
        x_measured = sem("x_measured")
        x1_ready = sem("x1_ready")
        x1_measured = sem("x1_measured")
        out_ready = sem("out_ready")
        x1_normed_ready = sem("x1_normed_ready")
        scores_made = sem("scores_made")
        max_ready = sem("max_ready")
        exp_ready = sem("exp_ready")
        inv_ready = sem("inv_ready")
        probs_ready = sem("probs_ready")
        probs_turned = sem("probs_turned")
        aggregated = sem("aggregated")
        stats_ready = sem("stats_ready")
        rstd_made = sem("rstd_made")
        norm_ready = sem("norm_ready")
        moments_seen = sem("moments_seen")
        norm_seen = sem("norm_seen")

        block = stack.enter_context(nc.Block())

        def norms_in(t):
            if isinstance(t, int):
                return slice(0 if t + 2 < PAIRS else 1, 2 if t >= 1 else 1)
            return slice(0, 2)

        @block.sync
        def _(sp):
            def load(t, par):
                if live(t - 1):
                    sp.wait_ge(x_measured, t - 1)
                sp.dma_start(x_all[:, t, :], x_pairs[:, t, :]).then_inc(x_loaded[par], 16)
                if live(t - 1):
                    sp.wait_ge(kv_made, t - 1)
                sp.dma_start(ctx_in[:, par, :], ctx_pairs[:, t, :]).then_inc(ctx_loaded[par], 16)

            def store(t):
                sp.wait_ge(out_ready, t + 1)
                sp.dma_start(out_pairs[:, t, :], x_all[:, t, :]).then_inc(stored, 16)

            load(0, 0)
            sp.dma_start(wk_sb[:, :], Wk).then_inc(w_loaded, 16)
            sp.dma_start(wq_sb[:, :], Wq).then_inc(w_loaded, 16)
            load(1, 1)
            for b in range(2):
                sp.dma_start(wv_twice[:, b, :], Wv).then_inc(w_loaded, 16)
                sp.dma_start(wskip_twice[:, b, :], Wskip).then_inc(w_loaded, 16)
            sp.dma_start(signs_raw[:, :, :], signs.rearrange("(k p) f -> p k f", p=P)).then_inc(signs_loaded, 16)
            LAG = 7
            for t in range(2, LAG):
                load(t, t % 2)
            with sp.Fori(LAG, PAIRS - 2, 2) as t:
                for odd in range(2):
                    load(t + odd, (LAG + odd) % 2)
                    store(t + odd - LAG)
            for t in range(PAIRS - 1, PAIRS):
                load(t, t % 2)
            for t in range(PAIRS - 1 - LAG, PAIRS):
                store(t)
            sp.wait_ge(stored, 16 * PAIRS)

        @block.tensor
        def _(pe):
            def kv(t, par):
                pe.wait_ge(ctx_loaded[par], 16 * (t // 2 + 1) if isinstance(t, int) else (t - par) * 8 + 16)
                if live(t):
                    pe.wait_ge(kv_ready, t)
                pe.matmul(ps_kv[:, 0, :], score_w[:, :], ctx_in[:, par, :], start=True, stop=True)
                pe.matmul(ps_kv[:, 1, :], ctx_in[:, par, :], value_w[:, :], start=True, stop=True).then_inc(kv_made, 1)

            def scores(t, b, par):
                if b == 0:
                    pe.wait_ge(up_ready, t + 1)
                    pe.wait_ge(kv_ready, t + 1)
                if live(2 * t + b - 1):
                    pe.wait_ge(exp_ready, 2 * t + b - 1)
                half = halves[b]
                for j in range(NT):
                    mm = pe.matmul(ps_scores[b][:, j, :], up[half, par, j * P:(j + 1) * P],
                                   keys_values[half, par, 0, :], start=True, stop=True)
                mm.then_inc(scores_made, 1)

            def values(t, par):
                pe.wait_ge(probs_t0_ready, t + 1)
                pe.wait_ge(probs_t1_ready, t + 1)
                for b, half in enumerate(halves):
                    mm = pe.matmul(ps_attn[half, :], keys_values[:, par, 1, half], probs_t[:, par, b, :],
                                   start=False, stop=True, skip_group_check=True)
                mm.then_inc(attn_made, 1)

            def ffn(t):
                pe.wait_ge(hi_ready, t + 1)
                pe.wait_ge(lo_ready, t + 1)
                if live(t):
                    pe.wait_ge(out_ready, t)
                for part in (turned_hi, turned_lo):
                    for k in range(NT):
                        mm = pe.matmul(ps_ffn[:, :], part[:, k, :], signs_sb[:, k, :],
                                       start=part is turned_hi and k == 0, stop=part is turned_lo and k == NT - 1)
                mm.then_inc(ffn_made, 1)

            def skip(t, par):
                if live(t):
                    pe.wait_ge(x1_ready, t)
                pe.matmul(ps_attn[:, :], skip_w[:, :], up[:, par, :], start=True, stop=False, skip_group_check=True)

            def turn_probs(t, b, par):
                pe.wait_ge(probs_ready, 2 * t + b + 1)
                for j in range(NT):
                    mm = pe.transpose(ps_probs_t[b][:, j * P:(j + 1) * P], probs[:, par, b, j, :], ident[:, :])
                mm.then_inc(probs_turned, 1)

            def turn_x1(t):
                pe.wait_ge(x1_normed_ready, t + 1)
                for k in range(NT):
                    mm = pe.transpose(ps_turned[:, k, :], x1_normed[:, k, :], ident[:, :])
                mm.then_inc(x1_turned, 1)

            def step(t, par, peeled=True):
                now = not peeled or 0 <= t < PAIRS
                before = not peeled or 1 <= t <= PAIRS
                if now:
                    scores(t, 0, par)
                if before:
                    turn_probs(t - 1, 1, 1 - par)
                if now:
                    scores(t, 1, par)
                if not peeled or t >= 3:
                    ffn(t - 3)
                if before:
                    values(t - 1, 1 - par)
                if not peeled or 2 <= t <= PAIRS + 1:
                    turn_x1(t - 2)
                if not peeled or t + 1 < PAIRS:
                    kv(t + 1, 1 - par)
                if now:
                    turn_probs(t, 0, par)
                    skip(t, par)

            pe.wait_ge(w_loaded, 16 * 6)
            for b, half in enumerate(halves):
                pe.matmul(ps_scores[0][half, 0, half], wk_sb[:, :], wq_sb[:, :], start=True, stop=True)
            pe.wait_ge(ident_ready, 2)
            pe.transpose(ps_scores[0][:, 1, 0:C], wskip_twice[:, :, :].rearrange("o b c -> o (b c)"), ident[0:C, 0:C])
            pe.transpose(ps_scores[0][:, 2, 0:C], wv_twice[:, :, :].rearrange("o b c -> o (b c)"),
                         ident[0:C, 0:C]).then_inc(w_products, 1)
            pe.wait_ge(w_ready, 1)
            kv(0, 0)
            for t in range(0, 3):
                step(t, t % 2)
            pe.wait_ge(signs_ready, 1)
            for t in range(3, 5):
                step(t, t % 2)
            with pe.Fori(5, PAIRS - 2, 2) as t:
                for odd in range(2):
                    step(t + odd, (1 + odd) % 2, peeled=False)
            for t in range(PAIRS - 1, PAIRS + 3):
                step(t, t % 2)

        @block.scalar
        def _(act):
            def head(t):
                act.wait_ge(x1_turned, t + 1)
                if live(t):
                    act.wait_ge(ffn_made, t)
                nc.scalar.activation(turned_hi[:, :, :], ps_turned[:, :, :], ACT.Copy).then_inc(hi_ready, 1)

            def exponentials(t, b, par):
                act.wait_ge(max_ready, 2 * t + b + 1)
                for j in range(NT):
                    last = nc.scalar.activation(probs[:, par, b, j, :], ps_scores[b][:, j, :], ACT.Exp,
                                                bias=minus_max[:, b, j:j + 1], accum_out=sums[:, b, j:j + 1])
                last.then_inc(exp_ready, 1)

            def copy_kv(t, par):
                act.wait_ge(kv_made, t + 1)
                if live(t - 1):
                    act.wait_ge(attn_made, t - 1)
                nc.scalar.activation(keys_values[:, par, :, :], ps_kv[:, 0:2, :], ACT.Copy).then_inc(kv_ready, 1)

            def normalize(t, par):
                act.wait_ge(norm_ready, t + 1)
                nc.scalar.activation(up[:, par, :], x_all[:, t, :], ACT.Identity, bias=shift[:, 0:1],
                                     scale=rstd[:, 0:1]).then_inc(up_ready, 1)

            def copy_probs(t, par):
                act.wait_ge(probs_turned, 2 * t + 1)
                if live(t - 1):
                    act.wait_ge(attn_made, t - 1)
                nc.scalar.activation(probs_t[:, par, 0, :], ps_probs_t[0][:, :], ACT.Copy).then_inc(probs_t0_ready, 1)

            def step(t, par, peeled=True):
                now = not peeled or 0 <= t < PAIRS
                if now:
                    exponentials(t, 0, par)
                    exponentials(t, 1, par)
                if not peeled or t + 1 < PAIRS:
                    normalize(t + 1, 1 - par)
                    copy_kv(t + 1, 1 - par)
                if not peeled or 2 <= t <= PAIRS + 1:
                    head(t - 2)
                if now:
                    copy_probs(t, par)

            act.dma_start(gates[:, 0:1], g_xattn[None, :].broadcast_to([P, 1])).then_inc(gates_loaded, 16)
            act.dma_start(gates[:, 1:2], g_ffn[None, :].broadcast_to([P, 1])).then_inc(gates_loaded, 16)
            act.dma_start(gates[:, 2:3], scale[None, :].broadcast_to([P, 1])).then_inc(gates_loaded, 16)
            act.wait_ge(gates_loaded, 48)
            nc.scalar.activation(tanh_gates[:, :], gates[:, 0:2], ACT.Tanh).then_inc(tanh_ready, 1)
            for t in range(-1, 3):
                step(t, t % 2)
            with act.Fori(3, PAIRS - 2, 2) as t:
                for odd in range(2):
                    step(t + odd, (1 + odd) % 2, peeled=False)
            for t in range(PAIRS - 1, PAIRS + 2):
                step(t, t % 2)

        @block.vector
        def _(dve):
            def rest(t):
                dve.wait_ge(hi_ready, t + 1)
                nc.vector.tensor_tensor(turned_lo[:, :, :], ps_turned[:, :, :], turned_hi[:, :, :],
                                        ALU.subtract).then_inc(lo_ready, 1)

            def maxima(t, b):
                dve.wait_ge(scores_made, 2 * t + b + 1)
                nc.vector.tensor_reduce(minus_max[:, b, :], ps_scores[b][:, :, :], AX_X, ALU.max,
                                        negate=True).then_inc(max_ready, 1)

            def measure_x(t, par):
                dve.wait_ge(x_loaded[par], 16 * (t // 2 + 1) if isinstance(t, int) else (t - par) * 8 + 16)
                nc.vector.bn_stats(moments[:, 0, :], x_all[:, t, :]).then_inc(x_measured, 1)

            def residual(t, par):
                if live(t - 1):
                    dve.wait_ge(out_ready, t - 1)
                dve.wait_ge(attn_made, t + 1)
                nc.vector.tensor_tensor(x1[:, par, :], ps_attn[:, :], x_all[:, t, :], ALU.add).then_inc(x1_ready, 1)

            def measure_x1(t, par):
                dve.wait_ge(x1_ready, t + 1)
                nc.vector.bn_stats(moments[:, 1, :], x1[:, par, :]).then_inc(x1_measured, 1)

            def statistics(t):
                cols = norms_in(t)
                if cols.start == 0:
                    dve.wait_ge(x_measured, t + 3)
                if cols.stop == 2:
                    dve.wait_ge(x1_measured, t)
                if live(t + 2):
                    dve.wait_ge(norm_ready, t + 2)
                dve.sem_inc(moments_seen, 1)
                if cols.start == 0:
                    last = nc.vector.bn_aggr(mean_var[:, 0, :], moments[:, 0, :])
                if cols.stop == 2:
                    last = nc.vector.bn_aggr(mean_var[:, 1, :], moments[:, 1, :])
                last.then_inc(aggregated, 1)
                dve.wait_ge(aggregated, t + 3)
                nc.vector.tensor_scalar(minus_mean[:, cols], mean_var[:, cols, 0], -1.0, None, ALU.mult)
                nc.vector.tensor_scalar(var_eps[:, cols], mean_var[:, cols, 1], EPS, None,
                                        ALU.add).then_inc(stats_ready, 1)

            def invert(t, b):
                if live(2 * t + b - 1):
                    dve.wait_ge(probs_ready, 2 * t + b - 1)
                dve.wait_ge(exp_ready, 2 * t + b + 1)
                nc.vector.reciprocal(inv_sums[:, b, :], sums[:, b, :]).then_inc(inv_ready, 1)

            def result(t, par):
                dve.wait_ge(ffn_made, t + 1)
                nc.vector.scalar_tensor_tensor(out=x_all[:, t, :], in0=ps_ffn[:, :], scalar=ffn_gain[:, 0:1],
                                               in1=x1[:, par, :], op0=ALU.mult, op1=ALU.add).then_inc(out_ready, 1)

            def copy_probs(t, par):
                dve.wait_ge(probs_turned, 2 * t + 2)
                if live(t - 1):
                    dve.wait_ge(attn_made, t - 1)
                nc.vector.tensor_copy(probs_t[:, par, 1, :], ps_probs_t[1][:, :]).then_inc(probs_t1_ready, 1)

            def step(t, par, peeled=True):
                now = not peeled or 0 <= t < PAIRS
                before = not peeled or 1 <= t <= PAIRS
                if now:
                    maxima(t, 0)
                if before:
                    copy_probs(t - 1, 1 - par)
                if now:
                    maxima(t, 1)
                    invert(t, 0)
                if not peeled or t + 2 < PAIRS:
                    measure_x(t + 2, par)
                if not peeled or t >= 3:
                    result(t - 3, 1 - par)
                if before:
                    residual(t - 1, 1 - par)
                if now:
                    invert(t, 1)
                if before:
                    measure_x1(t - 1, 1 - par)
                if not peeled or 2 <= t <= PAIRS + 1:
                    rest(t - 2)
                if not peeled or t <= PAIRS:
                    statistics(t)

            nc.vector.memset(minus_half[:, :], -0.5).then_inc(consts_set, 1)
            for w in (score_w, skip_w, value_w):
                nc.vector.memset(w[:, :], 0.0).then_inc(consts_set, 1)
            step(-2, 0)
            dve.wait_ge(tanh_ready, 1)
            nc.vector.tensor_tensor(ffn_gain[:, :], tanh_gates[:, 1:2], gates[:, 2:3], ALU.mult).then_inc(gain_ready, 1)
            dve.wait_ge(w_products, 1)
            dve.wait_ge(consts_set, 4)
            for half in halves:
                nc.vector.tensor_scalar(score_w[half, half], ps_scores[0][half, 0, half], float(C) ** -0.5, None,
                                        ALU.mult)
                nc.vector.tensor_scalar(skip_w[half, half], ps_scores[0][half, 1, 0:C], tanh_gates[half, 0:1], None,
                                        ALU.mult)
                last = nc.vector.tensor_scalar(value_w[half, half], ps_scores[0][half, 2, 0:C],
                                               tanh_gates[half, 0:1], None, ALU.mult)
            last.then_inc(w_ready, 1)
            dve.wait_ge(gain_ready, 1)
            for t in range(-1, 3):
                step(t, t % 2)
            with dve.Fori(3, PAIRS - 4, 2) as t:
                for odd in range(2):
                    step(t + odd, (1 + odd) % 2, peeled=False)
            for t in range(PAIRS - 3, PAIRS + 3):
                step(t, t % 2)

        @block.gpsimd
        def _(pool):
            def norm_factors(t):
                cols = norms_in(t)
                pool.wait_ge(stats_ready, t + 3)
                if live(t + 2) and (not isinstance(t, int) or t + 1 < PAIRS):
                    pool.wait_ge(up_ready, t + 2)
                nc.gpsimd.tensor_tensor(rstd[:, cols], var_eps[:, cols], minus_half[:, cols],
                                        ALU.pow).then_inc(rstd_made, 1)
                pool.wait_ge(rstd_made, t + 3)
                nc.gpsimd.tensor_tensor(shift[:, cols], minus_mean[:, cols], rstd[:, cols],
                                        ALU.mult).then_inc(norm_ready, 1)

            def normalize_x1(t, par):
                pool.wait_ge(norm_ready, t + 4)
                if live(t):
                    pool.wait_ge(x1_turned, t)
                pool.sem_inc(norm_seen, 1)
                nc.gpsimd.tensor_scalar(x1_normed[:, :, :].rearrange("p k n -> p (k n)"), x1[:, par, :],
                                        rstd[:, 1:2], shift[:, 1:2], ALU.mult, ALU.add).then_inc(x1_normed_ready, 1)

            def divide(t, b, par):
                pool.wait_ge(inv_ready, 2 * t + b + 1)
                nc.gpsimd.tensor_tensor(probs[:, par, b, :, :], probs[:, par, b, :, :],
                                        inv_sums[:, b, :, None].broadcast_to([P, NT, M]),
                                        ALU.mult).then_inc(probs_ready, 1)

            def step(t, par, peeled=True):
                if not peeled or 0 <= t < PAIRS:
                    divide(t, 0, par)
                    divide(t, 1, par)
                if not peeled or t <= PAIRS:
                    norm_factors(t)
                if not peeled or 1 <= t <= PAIRS:
                    normalize_x1(t - 1, 1 - par)

            nc.gpsimd.memset(ident[:, :], 0.0).then_inc(ident_ready, 1)
            pool.wait_ge(ident_ready, 1)
            nc.gpsimd.affine_select(out=ident[:, :], in_=ident[:, :], compare_op=ALU.not_equal, fill=1.0, base=0,
                                    pattern=[[-1, P]], channel_multiplier=1).then_inc(ident_ready, 1)
            pool.wait_ge(consts_set, 1)
            step(-2, 0)
            pool.wait_ge(signs_loaded, 16)
            for k in range(NT):
                last = nc.gpsimd.tensor_scalar(signs_sb[:, k, :], signs_raw[:, k, :], 2.0, -1.0, ALU.mult, ALU.add)
            last.then_inc(signs_ready, 1)
            for t in range(-1, 3):
                step(t, t % 2)
            with pool.Fori(3, PAIRS - 4, 2) as t:
                for odd in range(2):
                    step(t + odd, (1 + odd) % 2, peeled=False)
            for t in range(PAIRS - 3, PAIRS + 2):
                step(t, t % 2)


_INS = ["x", "ctx_1024", "g_xattn", "g_ffn", "L0_xattn_Wq", "L0_xattn_Wk", "L0_xattn_Wv", "L0_xattn_Wskip",
        "L0_ffn_kernel", "L0_ffn_scale"]


def kernel(**inputs):
    import numpy as np
    import concourse.bacc as bacc
    from concourse.bass_utils import run_bass_kernel_spmd as run

    nc = bacc.Bacc("TRN2", target_bir_lowering=False, num_devices=1)
    arrays, args = {}, []
    for name in _INS:
        a = np.ascontiguousarray(inputs[name])
        arrays[f"in_{name}"] = a
        args.append(nc.dram_tensor(f"in_{name}", a.shape, mybir.dt.from_np(a.dtype), kind="ExternalInput").ap())
    shape = inputs["x"].shape
    args.append(nc.dram_tensor("out", shape, F32, kind="ExternalOutput").ap())
    flamingo_gated_block(nc, *args)
    return run(nc, [arrays], core_ids=[0]).results[0]["out"]
```

```python
from contextlib import ExitStack

import concourse.bass as bass
from concourse import mybir

F32 = mybir.dt.float32
F16 = mybir.dt.float16
U8 = mybir.dt.uint8
ALU = mybir.AluOpType
ACT = mybir.ActivationFunctionType
AX_X = mybir.AxisListType.X
P = 128
EPS = 1e-5


def live(count):
    return not isinstance(count, int) or count > 0


def flamingo_gated_block(nc, x, ctx, g_xattn, g_ffn, Wq, Wk, Wv, Wskip, signs, scale, out):
    B, C, N = x.shape
    M = ctx.shape[2]
    PAIRS = B * C // P
    NT = N // P
    LAST = PAIRS - 1
    WARM_UP = 6
    assert 2 * C == P and M == P and N == 4 * P and PAIRS % 2 == 0 and PAIRS >= 8

    x_pairs = x.rearrange("(t b) c n -> (b c) t n", b=2)
    ctx_pairs = ctx.rearrange("(t b) c m -> (b c) t m", b=2)
    out_pairs = out.rearrange("(t b) c n -> (b c) t n", b=2)
    halves = [slice(0, C), slice(C, 2 * C)]

    with ExitStack() as stack:
        def sbuf(name, shape, dtype=F32):
            return stack.enter_context(nc.sbuf_tensor(name, shape, dtype))

        def bank(name, shape):
            return stack.enter_context(nc.psum_tensor(name, shape, F32))

        def sem(name):
            return stack.enter_context(nc.semaphore(name))

        ident = sbuf("ident", [P, P])
        minus_half = sbuf("minus_half", [P, 2])
        wq_sb = sbuf("wq_sb", [C, C])
        wk_sb = sbuf("wk_sb", [C, C])
        wskip_twice = sbuf("wskip_twice", [C, 2, C])
        wv_twice = sbuf("wv_twice", [C, 2, C])
        gates = sbuf("gates", [P, 4])
        tanh_gates = sbuf("tanh_gates", [P, 2])
        ffn_gain = sbuf("ffn_gain", [P, 1])
        signs_raw = sbuf("signs_raw", [P, NT, N], U8)
        signs_sb = sbuf("signs_sb", [P, NT, N], F16)
        score_w = sbuf("score_w", [P, P])
        skip_w = sbuf("skip_w", [P, P])
        value_w = sbuf("value_w", [P, P])
        x_all = sbuf("x_all", [P, PAIRS, N])
        ctx_in = sbuf("ctx_in", [P, 2, M])
        keys_values = sbuf("keys_values", [P, 2, 2, P])
        up = sbuf("up", [P, 2, N])
        x1 = sbuf("x1", [P, 5, N])
        minus_max = sbuf("minus_max", [P, 2, NT])
        sums = sbuf("sums", [P, 2, NT])
        inv_sums = sbuf("inv_sums", [P, 2, NT])
        probs = sbuf("probs", [P, 2, 2, NT, M])
        probs_t = sbuf("probs_t", [P, 2, 2, N])
        moments = sbuf("moments", [P, 2, 6])
        mean_var = sbuf("mean_var", [P, 2, 2])
        var_eps = sbuf("var_eps", [P, 2])
        minus_mean = sbuf("minus_mean", [P, 2])
        rstd = sbuf("rstd", [P, 2])
        shift = sbuf("shift", [P, 2])
        x1_normed = sbuf("x1_normed", [P, NT, P])
        turned_hi = sbuf("turned_hi", [P, 2, NT, P], F16)
        turned_lo = sbuf("turned_lo", [P, 2, NT, P], F16)

        ps_scores = [bank(f"ps_scores{b}", [P, NT, M]) for b in range(2)]
        ps_probs_t = [bank(f"ps_probs_t{b}", [P, N]) for b in range(2)]
        ps_attn = bank("ps_attn", [P, N])
        ps_turned = bank("ps_turned", [P, NT, P])
        ps_ffn = bank("ps_ffn", [P, N])
        ps_kv = bank("ps_kv", [P, 4, P])

        scores_banks = [b[:, :, :].rearrange("p k m -> p (k m)") for b in ps_scores]
        kv_bank = ps_kv[:, :, :].rearrange("p k m -> p (k m)")
        late_turned = ps_probs_t[0][:, :].rearrange("p (k m) -> p k m", k=NT)
        last_halves = [(slice(0, N // 2), kv_bank), (slice(N // 2, N), ps_ffn)]
        setup_banks = [b[:, 0, :] for b in (ps_scores[0], ps_turned)] + [ps_probs_t[1][:, 0:C]]

        score_w_loaded = sem("score_w_loaded")
        w_loaded = sem("w_loaded")
        gates_loaded = sem("gates_loaded")
        signs_loaded = sem("signs_loaded")
        x_loaded = [sem(f"x_loaded{k}") for k in range(2)]
        ctx_loaded = [sem(f"ctx_loaded{k}") for k in range(2)]
        stored = sem("stored")
        consts_set = sem("consts_set")
        ident_ready = sem("ident_ready")
        tanh_ready = sem("tanh_ready")
        gain_ready = sem("gain_ready")
        w_products = sem("w_products")
        w_ready = sem("w_ready")
        first_keys_made = sem("first_keys_made")
        first_keys_ready = sem("first_keys_ready")
        signs_ready = sem("signs_ready")
        kv_made = sem("kv_made")
        attn_made = sem("attn_made")
        ffn_made = sem("ffn_made")
        x1_turned = sem("x1_turned")
        kv_ready = sem("kv_ready")
        up_ready = sem("up_ready")
        hi_ready = sem("hi_ready")
        probs_t0_ready = sem("probs_t0_ready")
        probs_t1_ready = sem("probs_t1_ready")
        lo_ready = sem("lo_ready")
        x_measured = sem("x_measured")
        x1_ready = sem("x1_ready")
        x1_measured = sem("x1_measured")
        out_ready = sem("out_ready")
        x1_normed_ready = sem("x1_normed_ready")
        scores_made = sem("scores_made")
        max_ready = sem("max_ready")
        exp_ready = sem("exp_ready")
        inv_ready = sem("inv_ready")
        probs_ready = sem("probs_ready")
        probs_turned = sem("probs_turned")
        aggregated = sem("aggregated")
        stats_ready = sem("stats_ready")
        rstd_made = sem("rstd_made")
        norm_ready = sem("norm_ready")
        moments_seen = sem("moments_seen")
        norm_seen = sem("norm_seen")

        block = stack.enter_context(nc.Block())

        def norms_in(t):
            if isinstance(t, int):
                return slice(0 if t + 2 < PAIRS else 1, 2 if t >= 1 else 1)
            return slice(0, 2)

        @block.sync
        def _(sp):
            def load_x(t, par):
                if live(t - 1):
                    sp.wait_ge(x_measured, t - 1)
                sp.dma_start(x_all[:, t, :], x_pairs[:, t, :]).then_inc(x_loaded[par], 16)

            def load_ctx(t, par):
                if live(t - 1):
                    sp.wait_ge(kv_made, t - 1)
                sp.dma_start(ctx_in[:, par, :], ctx_pairs[:, t, :]).then_inc(ctx_loaded[par], 16)

            def load(t, par):
                load_x(t, par)
                load_ctx(t, par)

            def store(t):
                sp.wait_ge(out_ready, t + 1)
                sp.dma_start(out_pairs[:, t, :], x_all[:, t, :]).then_inc(stored, 16)

            load_x(0, 0)
            sp.dma_start(wk_sb[:, :], Wk).then_inc(score_w_loaded, 16)
            sp.dma_start(wq_sb[:, :], Wq).then_inc(score_w_loaded, 16)
            load_ctx(0, 0)
            load_x(1, 1)
            twice = [C, 2, C]
            sp.dma_start(wv_twice[:, :, :], Wv[:, None, :].broadcast_to(twice)).then_inc(w_loaded, 16)
            sp.dma_start(wskip_twice[:, :, :], Wskip[:, None, :].broadcast_to(twice)).then_inc(w_loaded, 16)
            load_ctx(1, 1)
            sp.dma_start(signs_raw[:, :, :], signs.rearrange("(k p) f -> p k f", p=P)).then_inc(signs_loaded, 16)
            LAG = 7
            for t in range(2, LAG):
                load(t, t % 2)
            with sp.Fori(LAG, PAIRS - 2, 2) as t:
                for odd in range(2):
                    load(t + odd, (LAG + odd) % 2)
                    store(t + odd - LAG)
            for t in range(PAIRS - 1, PAIRS):
                load(t, t % 2)
            for t in range(LAST - LAG, LAST):
                store(t)
            for k, (cols, _) in enumerate(last_halves):
                sp.wait_ge(out_ready, LAST + 1 + k)
                sp.dma_start(out_pairs[:, LAST, cols], x_all[:, LAST, cols]).then_inc(stored, 16)
            sp.wait_ge(stored, 16 * (PAIRS + 1))

        @block.tensor
        def _(pe):
            def kv(t, par):
                pe.wait_ge(ctx_loaded[par], 16 * (t // 2 + 1) if isinstance(t, int) else (t - par) * 8 + 16)
                if live(t):
                    pe.wait_ge(kv_ready, t)
                pe.matmul(ps_kv[:, 0, :], score_w[:, :], ctx_in[:, par, :], start=True, stop=True)
                pe.matmul(ps_kv[:, 1, :], ctx_in[:, par, :], value_w[:, :], start=True, stop=True).then_inc(kv_made, 1)

            def first_keys():
                pe.wait_ge(ctx_loaded[0], 16)
                pe.wait_ge(w_ready, 1)
                pe.matmul(ps_kv[:, 0, :], score_w[:, :], ctx_in[:, 0, :], start=True, stop=True).then_inc(first_keys_made, 1)

            def first_values():
                pe.wait_ge(w_ready, 2)
                pe.matmul(ps_kv[:, 1, :], ctx_in[:, 0, :], value_w[:, :], start=True, stop=True).then_inc(kv_made, 1)

            def keep_warm(count):
                for _ in range(count):
                    pe.matmul(ps_ffn[:, 0:P], ident[:, :], ident[:, :], start=True, stop=True)

            def scores(t, b, par):
                if b == 0:
                    pe.wait_ge(up_ready, t + 1)
                    if live(t):
                        pe.wait_ge(kv_ready, t + 1)
                    else:
                        pe.wait_ge(first_keys_ready, 1)
                if live(2 * t + b - 1):
                    pe.wait_ge(exp_ready, 2 * t + b - 1)
                half = halves[b]
                for j in range(NT):
                    mm = pe.matmul(ps_scores[b][:, j, :], up[half, par, j * P:(j + 1) * P],
                                   keys_values[half, par, 0, :], start=True, stop=True)
                mm.then_inc(scores_made, 1)

            def pair_scores(t, par):
                pe.wait_ge(up_ready, t + 1)
                pe.wait_ge(kv_ready, t + 1)
                pe.wait_ge(exp_ready, 2 * t)
                for j in range(NT):
                    for b, half in enumerate(halves):
                        mm = pe.matmul(ps_scores[b][:, j, :], up[half, par, j * P:(j + 1) * P],
                                       keys_values[half, par, 0, :], start=True, stop=True)
                mm.then_inc(scores_made, 2)

            def values(t, par):
                pe.wait_ge(probs_t0_ready, t + 1)
                pe.wait_ge(probs_t1_ready, t + 1)
                for b, half in enumerate(halves):
                    mm = pe.matmul(ps_attn[half, :], keys_values[:, par, 1, half], probs_t[:, par, b, :],
                                   start=False, stop=True, skip_group_check=True)
                mm.then_inc(attn_made, 1)

            def ffn_part(t, par, part, sums_to, cols=slice(0, N)):
                turned, ready = ((turned_hi, hi_ready), (turned_lo, lo_ready))[part]
                pe.wait_ge(ready, t + 1)
                for k in range(NT):
                    mm = pe.matmul(sums_to[:, cols], turned[:, par, k, :], signs_sb[:, k, cols],
                                   start=part == 0 and k == 0, stop=part == 1 and k == NT - 1)
                if part == 1:
                    mm.then_inc(ffn_made, 1)

            def ffn(t, par):
                if live(t):
                    pe.wait_ge(out_ready, t)
                ffn_part(t, par, 0, ps_ffn)
                ffn_part(t, par, 1, ps_ffn)

            def skip(t, par):
                if live(t):
                    pe.wait_ge(x1_ready, t)
                pe.matmul(ps_attn[:, :], skip_w[:, :], up[:, par, :], start=True, stop=False, skip_group_check=True)

            def turn_probs(t, b, par):
                pe.wait_ge(probs_ready, 2 * t + b + 1)
                for j in range(NT):
                    mm = pe.transpose(ps_probs_t[b][:, j * P:(j + 1) * P], probs[:, par, b, j, :], ident[:, :])
                mm.then_inc(probs_turned, 1)

            def turn_x1(t, turned=ps_turned):
                pe.wait_ge(x1_normed_ready, t + 1)
                for k in range(NT):
                    mm = pe.transpose(turned[:, k, :], x1_normed[:, k, :], ident[:, :])
                mm.then_inc(x1_turned, 1)

            def rest_of_step(t, par, with_ffn=True):
                if with_ffn:
                    ffn(t - 3, 1 - par)
                values(t - 1, 1 - par)
                turn_x1(t - 2)
                kv(t + 1, 1 - par)
                turn_probs(t, 0, par)
                skip(t, par)

            def step(t, par):
                pair_scores(t, par)
                turn_probs(t - 1, 1, 1 - par)
                rest_of_step(t, par)

            pe.wait_ge(ident_ready, 2)
            keep_warm(WARM_UP)
            pe.wait_ge(score_w_loaded, 32)
            for b, half in enumerate(halves):
                mm = pe.matmul(setup_banks[0][half, half], wk_sb[:, :], wq_sb[:, :], start=True, stop=True)
            mm.then_inc(w_products, 1)
            keep_warm(2)
            first_keys()
            keep_warm(1)
            pe.wait_ge(w_loaded, 32)
            for k, w in ((1, wv_twice), (2, wskip_twice)):
                pe.transpose(setup_banks[k][:, 0:C], w[:, :, :].rearrange("o b c -> o (b c)"),
                             ident[0:C, 0:C]).then_inc(w_products, 1)
            scores(0, 0, 0)
            scores(0, 1, 0)
            first_values()
            pe.wait_ge(w_ready, 3)
            skip(0, 0)
            kv(1, 1)
            scores(1, 0, 1)
            turn_probs(0, 0, 0)
            scores(1, 1, 1)
            turn_probs(0, 1, 0)
            kv(2, 0)
            values(0, 0)
            turn_probs(1, 0, 1)
            skip(1, 1)
            scores(2, 0, 0)
            turn_probs(1, 1, 1)
            scores(2, 1, 0)
            rest_of_step(2, 0, with_ffn=False)
            pe.wait_ge(signs_ready, 1)
            for t in range(3, 5):
                step(t, t % 2)
            with pe.Fori(5, PAIRS - 4, 2) as t:
                for odd in range(2):
                    step(t + odd, (1 + odd) % 2)
            step(LAST - 2, 1)
            scores(LAST - 1, 0, 0)
            turn_probs(LAST - 2, 1, 1)
            scores(LAST - 1, 1, 0)
            values(LAST - 2, 1)
            turn_x1(LAST - 3)
            kv(LAST, 1)
            turn_probs(LAST - 1, 0, 0)
            skip(LAST - 1, 0)
            scores(LAST, 0, 1)
            turn_probs(LAST - 1, 1, 0)
            scores(LAST, 1, 1)
            ffn(LAST - 4, 1)
            values(LAST - 1, 0)
            turn_probs(LAST, 0, 1)
            pe.wait_ge(out_ready, LAST - 3)
            ffn_part(LAST - 3, 0, 0, ps_ffn)
            turn_probs(LAST, 1, 1)
            skip(LAST, 1)
            values(LAST, 1)
            turn_x1(LAST - 2)
            ffn_part(LAST - 3, 0, 1, ps_ffn)
            ffn_part(LAST - 2, 1, 0, scores_banks[0])
            turn_x1(LAST - 1, late_turned)
            ffn_part(LAST - 2, 1, 1, scores_banks[0])
            turn_x1(LAST)
            ffn_part(LAST - 1, 0, 0, scores_banks[1])
            ffn_part(LAST - 1, 0, 1, scores_banks[1])
            pe.wait_ge(out_ready, LAST - 2)
            for part in range(2):
                for cols, sums_to in last_halves:
                    ffn_part(LAST, 1, part, sums_to, cols)

        @block.scalar
        def _(act):
            def head(t, par, turned=ps_turned):
                act.wait_ge(x1_turned, t + 1)
                if live(t - 1):
                    act.wait_ge(ffn_made, t - 1)
                nc.scalar.activation(turned_hi[:, par, :, :], turned[:, :, :], ACT.Copy).then_inc(hi_ready, 1)

            def exponentials(t, b, par):
                act.wait_ge(max_ready, 2 * t + b + 1)
                for j in range(NT):
                    last = nc.scalar.activation(probs[:, par, b, j, :], ps_scores[b][:, j, :], ACT.Exp,
                                                bias=minus_max[:, b, j:j + 1], accum_out=sums[:, b, j:j + 1])
                last.then_inc(exp_ready, 1)

            def copy_kv(t, par):
                act.wait_ge(kv_made, t + 1)
                if live(t - 1):
                    act.wait_ge(attn_made, t - 1)
                nc.scalar.activation(keys_values[:, par, :, :], ps_kv[:, 0:2, :], ACT.Copy).then_inc(kv_ready, 1)

            def normalize(t, par):
                act.wait_ge(norm_ready, t + 1)
                nc.scalar.activation(up[:, par, :], x_all[:, t, :], ACT.Identity, bias=shift[:, 0:1],
                                     scale=rstd[:, 0:1]).then_inc(up_ready, 1)

            def copy_probs(t, par):
                act.wait_ge(probs_turned, 2 * t + 1)
                if live(t - 1):
                    act.wait_ge(attn_made, t - 1)
                nc.scalar.activation(probs_t[:, par, 0, :], ps_probs_t[0][:, :], ACT.Copy).then_inc(probs_t0_ready, 1)

            def step(t, par):
                exponentials(t, 0, par)
                exponentials(t, 1, par)
                normalize(t + 1, 1 - par)
                copy_kv(t + 1, 1 - par)
                head(t - 2, par)
                copy_probs(t, par)

            normalize(0, 0)
            act.wait_ge(first_keys_made, 1)
            nc.scalar.activation(keys_values[:, 0, 0, :], ps_kv[:, 0, :], ACT.Copy).then_inc(first_keys_ready, 1)
            act.wait_ge(gates_loaded, 48)
            nc.scalar.activation(tanh_gates[:, :], gates[:, 0:2], ACT.Tanh).then_inc(tanh_ready, 1)
            normalize(1, 1)
            exponentials(0, 0, 0)
            act.wait_ge(kv_made, 1)
            nc.scalar.activation(keys_values[:, 0, 1, :], ps_kv[:, 1, :], ACT.Copy).then_inc(kv_ready, 1)
            copy_kv(1, 1)
            exponentials(0, 1, 0)
            normalize(2, 0)
            copy_probs(0, 0)
            exponentials(1, 0, 1)
            exponentials(1, 1, 1)
            copy_kv(2, 0)
            copy_probs(1, 1)
            step(2, 0)
            with act.Fori(3, PAIRS - 4, 2) as t:
                for odd in range(2):
                    step(t + odd, (1 + odd) % 2)
            for t in range(LAST - 2, LAST):
                step(t, t % 2)
            exponentials(LAST, 0, 1)
            exponentials(LAST, 1, 1)
            copy_probs(LAST, 1)
            head(LAST - 2, 1)
            head(LAST - 1, 0, late_turned)
            head(LAST, 1)

        @block.vector
        def _(dve):
            def rest(t, par, turned=ps_turned):
                dve.wait_ge(hi_ready, t + 1)
                nc.vector.tensor_tensor(turned_lo[:, par, :, :], turned[:, :, :], turned_hi[:, par, :, :],
                                        ALU.subtract).then_inc(lo_ready, 1)

            def maxima(t, b):
                dve.wait_ge(scores_made, 2 * t + b + 1)
                nc.vector.tensor_reduce(minus_max[:, b, :], ps_scores[b][:, :, :], AX_X, ALU.max,
                                        negate=True).then_inc(max_ready, 1)

            def measure_x(t, par):
                dve.wait_ge(x_loaded[par], 16 * (t // 2 + 1) if isinstance(t, int) else (t - par) * 8 + 16)
                nc.vector.bn_stats(moments[:, 0, :], x_all[:, t, :]).then_inc(x_measured, 1)

            def residual(t, slot):
                if live(t - 1) and slot < 2:
                    dve.wait_ge(out_ready, t - 1)
                dve.wait_ge(attn_made, t + 1)
                nc.vector.tensor_tensor(x1[:, slot, :], ps_attn[:, :], x_all[:, t, :], ALU.add).then_inc(x1_ready, 1)

            def measure_x1(t, slot):
                dve.wait_ge(x1_ready, t + 1)
                nc.vector.bn_stats(moments[:, 1, :], x1[:, slot, :]).then_inc(x1_measured, 1)

            def statistics(t):
                cols = norms_in(t)
                if cols.start == 0:
                    dve.wait_ge(x_measured, t + 3)
                if cols.stop == 2:
                    dve.wait_ge(x1_measured, t)
                if live(t + 2):
                    dve.wait_ge(norm_ready, t + 2)
                dve.sem_inc(moments_seen, 1)
                if cols.start == 0:
                    last = nc.vector.bn_aggr(mean_var[:, 0, :], moments[:, 0, :])
                if cols.stop == 2:
                    last = nc.vector.bn_aggr(mean_var[:, 1, :], moments[:, 1, :])
                last.then_inc(aggregated, 1)
                dve.wait_ge(aggregated, t + 3)
                nc.vector.tensor_scalar(minus_mean[:, cols], mean_var[:, cols, 0], -1.0, None, ALU.mult)
                nc.vector.tensor_scalar(var_eps[:, cols], mean_var[:, cols, 1], EPS, None,
                                        ALU.add).then_inc(stats_ready, 1)

            def invert(t, b):
                if live(2 * t + b - 1):
                    dve.wait_ge(probs_ready, 2 * t + b - 1)
                dve.wait_ge(exp_ready, 2 * t + b + 1)
                nc.vector.reciprocal(inv_sums[:, b, :], sums[:, b, :]).then_inc(inv_ready, 1)

            def result(t, slot, product=ps_ffn):
                dve.wait_ge(ffn_made, t + 1)
                nc.vector.scalar_tensor_tensor(out=x_all[:, t, :], in0=product[:, :], scalar=ffn_gain[:, 0:1],
                                               in1=x1[:, slot, :], op0=ALU.mult, op1=ALU.add).then_inc(out_ready, 1)

            def copy_probs(t, par):
                dve.wait_ge(probs_turned, 2 * t + 2)
                if live(t - 1):
                    dve.wait_ge(attn_made, t - 1)
                nc.vector.tensor_copy(probs_t[:, par, 1, :], ps_probs_t[1][:, :]).then_inc(probs_t1_ready, 1)

            def step(t, par, with_result=True):
                maxima(t, 0)
                copy_probs(t - 1, 1 - par)
                maxima(t, 1)
                invert(t, 0)
                if with_result:
                    result(t - 3, 1 - par)
                residual(t - 1, 1 - par)
                invert(t, 1)
                measure_x1(t - 1, 1 - par)
                measure_x(t + 2, par)
                rest(t - 2, par)
                statistics(t)

            def block_diagonal(w, k):
                dve.wait_ge(w_products, k + 1)
                for half in halves:
                    last = nc.vector.tensor_scalar(w[half, half], setup_banks[k][half, half if k == 0 else slice(0, C)],
                                                   tanh_gates[half, 0:1] if k else float(C) ** -0.5, None, ALU.mult)
                last.then_inc(w_ready, 1)

            nc.vector.memset(minus_half[:, :], -0.5).then_inc(consts_set, 1)
            for w in (score_w, skip_w, value_w):
                nc.vector.memset(w[:, :], 0.0).then_inc(consts_set, 1)
            measure_x(0, 0)
            statistics(-2)
            dve.wait_ge(consts_set, 4)
            block_diagonal(score_w, 0)
            measure_x(1, 1)
            statistics(-1)
            dve.wait_ge(tanh_ready, 1)
            nc.vector.tensor_tensor(ffn_gain[:, :], tanh_gates[:, 1:2], gates[:, 2:3], ALU.mult).then_inc(gain_ready, 1)
            block_diagonal(value_w, 1)
            maxima(0, 0)
            block_diagonal(skip_w, 2)
            dve.wait_ge(gain_ready, 1)
            maxima(0, 1)
            measure_x(2, 0)
            statistics(0)
            invert(0, 0)
            invert(0, 1)
            maxima(1, 0)
            maxima(1, 1)
            copy_probs(0, 0)
            invert(1, 0)
            measure_x(3, 1)
            residual(0, 0)
            invert(1, 1)
            measure_x1(0, 0)
            statistics(1)
            step(2, 0, with_result=False)
            with dve.Fori(3, PAIRS - 4, 2) as t:
                for odd in range(2):
                    step(t + odd, (1 + odd) % 2)
            step(LAST - 2, 1)
            maxima(LAST - 1, 0)
            copy_probs(LAST - 2, 1)
            maxima(LAST - 1, 1)
            invert(LAST - 1, 0)
            residual(LAST - 2, 2)
            invert(LAST - 1, 1)
            measure_x1(LAST - 2, 2)
            rest(LAST - 3, 0)
            statistics(LAST - 1)
            maxima(LAST, 0)
            copy_probs(LAST - 1, 0)
            maxima(LAST, 1)
            invert(LAST, 0)
            result(LAST - 4, 1)
            invert(LAST, 1)
            residual(LAST - 1, 3)
            measure_x1(LAST - 1, 3)
            statistics(LAST)
            copy_probs(LAST, 1)
            residual(LAST, 4)
            measure_x1(LAST, 4)
            statistics(LAST + 1)
            rest(LAST - 2, 1)
            result(LAST - 3, 0)
            dve.wait_ge(norm_ready, LAST + 4)
            dve.wait_ge(x1_turned, LAST)
            nc.vector.tensor_scalar(x1_normed[:, :, :].rearrange("p k n -> p (k n)"), x1[:, 4, :], rstd[:, 1:2],
                                    shift[:, 1:2], ALU.mult, ALU.add).then_inc(x1_normed_ready, 1)
            rest(LAST - 1, 0, late_turned)
            result(LAST - 2, 2, scores_banks[0])
            rest(LAST, 1)
            result(LAST - 1, 3, scores_banks[1])
            for k, (cols, product) in enumerate(last_halves):
                dve.wait_ge(ffn_made, LAST + 1 + k)
                nc.vector.scalar_tensor_tensor(out=x_all[:, LAST, cols], in0=product[:, cols],
                                               scalar=ffn_gain[:, 0:1], in1=x1[:, 4, cols], op0=ALU.mult,
                                               op1=ALU.add).then_inc(out_ready, 1)

        @block.gpsimd
        def _(pool):
            def norm_factors(t):
                cols = norms_in(t)
                pool.wait_ge(stats_ready, t + 3)
                if live(t + 2) and (not isinstance(t, int) or t + 1 < PAIRS):
                    pool.wait_ge(up_ready, t + 2)
                nc.gpsimd.tensor_tensor(rstd[:, cols], var_eps[:, cols], minus_half[:, cols],
                                        ALU.pow).then_inc(rstd_made, 1)
                pool.wait_ge(rstd_made, t + 3)
                nc.gpsimd.tensor_tensor(shift[:, cols], minus_mean[:, cols], rstd[:, cols],
                                        ALU.mult).then_inc(norm_ready, 1)

            def normalize_x1(t, slot):
                pool.wait_ge(norm_ready, t + 4)
                if live(t):
                    pool.wait_ge(x1_turned, t)
                pool.sem_inc(norm_seen, 1)
                nc.gpsimd.tensor_scalar(x1_normed[:, :, :].rearrange("p k n -> p (k n)"), x1[:, slot, :],
                                        rstd[:, 1:2], shift[:, 1:2], ALU.mult, ALU.add).then_inc(x1_normed_ready, 1)

            def divide(t, b, par):
                pool.wait_ge(inv_ready, 2 * t + b + 1)
                nc.gpsimd.tensor_tensor(probs[:, par, b, :, :], probs[:, par, b, :, :],
                                        inv_sums[:, b, :, None].broadcast_to([P, NT, M]),
                                        ALU.mult).then_inc(probs_ready, 1)

            def step(t, par):
                divide(t, 0, par)
                divide(t, 1, par)
                norm_factors(t)
                normalize_x1(t - 1, 1 - par)

            nc.gpsimd.memset(ident[:, :], 0.0).then_inc(ident_ready, 1)
            pool.wait_ge(ident_ready, 1)
            nc.gpsimd.affine_select(out=ident[:, :], in_=ident[:, :], compare_op=ALU.not_equal, fill=1.0, base=0,
                                    pattern=[[-1, P]], channel_multiplier=1).then_inc(ident_ready, 1)
            for k, scalar in enumerate((g_xattn, g_ffn, scale)):
                pool.dma_start(gates[:, k:k + 1], scalar[None, :].broadcast_to([P, 1])).then_inc(gates_loaded, 16)
            pool.wait_ge(consts_set, 1)
            norm_factors(-2)
            norm_factors(-1)
            pool.wait_ge(signs_loaded, 16)
            for k in range(NT):
                last = nc.gpsimd.tensor_scalar(signs_sb[:, k, :], signs_raw[:, k, :], 2.0, -1.0, ALU.mult, ALU.add)
            last.then_inc(signs_ready, 1)
            norm_factors(0)
            divide(0, 0, 0)
            divide(0, 1, 0)
            step(1, 1)
            step(2, 0)
            with pool.Fori(3, PAIRS - 4, 2) as t:
                for odd in range(2):
                    step(t + odd, (1 + odd) % 2)
            step(LAST - 2, 1)
            for t in (LAST - 1, LAST):
                divide(t, 0, t % 2)
                divide(t, 1, t % 2)
                pool.wait_ge(x1_normed_ready, t - 1)
                norm_factors(t)
                normalize_x1(t - 1, t + 3 - LAST)
            pool.wait_ge(x1_normed_ready, LAST)
            norm_factors(LAST + 1)


_INS = ["x", "ctx_1024", "g_xattn", "g_ffn", "L0_xattn_Wq", "L0_xattn_Wk", "L0_xattn_Wv", "L0_xattn_Wskip",
        "L0_ffn_kernel", "L0_ffn_scale"]


def kernel(**inputs):
    import numpy as np
    import concourse.bacc as bacc
    from concourse.bass_utils import run_bass_kernel_spmd as run

    nc = bacc.Bacc("TRN2", target_bir_lowering=False, num_devices=1)
    arrays, args = {}, []
    for name in _INS:
        a = np.ascontiguousarray(inputs[name])
        arrays[f"in_{name}"] = a
        args.append(nc.dram_tensor(f"in_{name}", a.shape, mybir.dt.from_np(a.dtype), kind="ExternalInput").ap())
    shape = inputs["x"].shape
    args.append(nc.dram_tensor("out", shape, F32, kind="ExternalOutput").ap())
    flamingo_gated_block(nc, *args)
    return run(nc, [arrays], core_ids=[0]).results[0]["out"]
```
